# Optimizing a Trainium2 kernel written in Bass

```python
import numpy as np
import jax
import jax.numpy as jnp

def _softmax(x, axis=-1):
    return jax.nn.softmax(x, axis=axis)

def _gelu(x):
    return jax.nn.gelu(x, approximate=True)

def _silu(x):
    return jax.nn.silu(x)

def _sigmoid(x):
    return jax.nn.sigmoid(x)

def _layernorm(x, axis=-1, eps=1e-05):
    m = jnp.mean(x, axis=axis, keepdims=True)
    v = jnp.var(x, axis=axis, keepdims=True)
    return (x - m) / jnp.sqrt(v + eps)

def _scatter_add(tgt, idx, src, axis=0):
    return tgt.at[idx].add(src)

def _segment_sum(src, seg, n):
    return jax.ops.segment_sum(src, seg, n)
kernel_name = 'mk_dlrm_tower_d1_rec_r8_60d7e8'

def setup_inputs(seed: int=0):
    np.random.seed(seed)
    _w = jnp.asarray

    def _rec_inputs():
        import jax
        import jax.numpy as jnp
        _tk = jax.random.key(seed)
        ids = jnp.stack([jax.random.randint(jax.random.fold_in(_tk, 200 + f), (512,), 0, v, jnp.int32) for f, v in enumerate([1000, 125000, 1250, 12500, 1000, 1250, 1250, 12500, 1000, 1000, 1000, 1000, 1250, 1000, 1000, 12500, 12500, 1250, 1000, 1250, 1250, 12500, 1250, 12500, 1000, 1250])], axis=1)
        tbl_0 = 0.05 * jax.random.normal(jax.random.fold_in(_tk, 500 + 0), (1000, 128), jnp.float32)
        tbl_1 = 0.05 * jax.random.normal(jax.random.fold_in(_tk, 500 + 1), (125000, 128), jnp.float32)
        tbl_2 = 0.05 * jax.random.normal(jax.random.fold_in(_tk, 500 + 2), (1250, 128), jnp.float32)
        tbl_3 = 0.05 * jax.random.normal(jax.random.fold_in(_tk, 500 + 3), (12500, 128), jnp.float32)
        tbl_4 = 0.05 * jax.random.normal(jax.random.fold_in(_tk, 500 + 4), (1000, 128), jnp.float32)
        tbl_5 = 0.05 * jax.random.normal(jax.random.fold_in(_tk, 500 + 5), (1250, 128), jnp.float32)
        tbl_6 = 0.05 * jax.random.normal(jax.random.fold_in(_tk, 500 + 6), (1250, 128), jnp.float32)
        tbl_7 = 0.05 * jax.random.normal(jax.random.fold_in(_tk, 500 + 7), (12500, 128), jnp.float32)
        tbl_8 = 0.05 * jax.random.normal(jax.random.fold_in(_tk, 500 + 8), (1000, 128), jnp.float32)
        tbl_9 = 0.05 * jax.random.normal(jax.random.fold_in(_tk, 500 + 9), (1000, 128), jnp.float32)
        tbl_10 = 0.05 * jax.random.normal(jax.random.fold_in(_tk, 500 + 10), (1000, 128), jnp.float32)
        tbl_11 = 0.05 * jax.random.normal(jax.random.fold_in(_tk, 500 + 11), (1000, 128), jnp.float32)
        tbl_12 = 0.05 * jax.random.normal(jax.random.fold_in(_tk, 500 + 12), (1250, 128), jnp.float32)
        tbl_13 = 0.05 * jax.random.normal(jax.random.fold_in(_tk, 500 + 13), (1000, 128), jnp.float32)
        tbl_14 = 0.05 * jax.random.normal(jax.random.fold_in(_tk, 500 + 14), (1000, 128), jnp.float32)
        tbl_15 = 0.05 * jax.random.normal(jax.random.fold_in(_tk, 500 + 15), (12500, 128), jnp.float32)
        tbl_16 = 0.05 * jax.random.normal(jax.random.fold_in(_tk, 500 + 16), (12500, 128), jnp.float32)
        tbl_17 = 0.05 * jax.random.normal(jax.random.fold_in(_tk, 500 + 17), (1250, 128), jnp.float32)
        tbl_18 = 0.05 * jax.random.normal(jax.random.fold_in(_tk, 500 + 18), (1000, 128), jnp.float32)
        tbl_19 = 0.05 * jax.random.normal(jax.random.fold_in(_tk, 500 + 19), (1250, 128), jnp.float32)
        tbl_20 = 0.05 * jax.random.normal(jax.random.fold_in(_tk, 500 + 20), (1250, 128), jnp.float32)
        tbl_21 = 0.05 * jax.random.normal(jax.random.fold_in(_tk, 500 + 21), (12500, 128), jnp.float32)
        tbl_22 = 0.05 * jax.random.normal(jax.random.fold_in(_tk, 500 + 22), (1250, 128), jnp.float32)
        tbl_23 = 0.05 * jax.random.normal(jax.random.fold_in(_tk, 500 + 23), (12500, 128), jnp.float32)
        tbl_24 = 0.05 * jax.random.normal(jax.random.fold_in(_tk, 500 + 24), (1000, 128), jnp.float32)
        tbl_25 = 0.05 * jax.random.normal(jax.random.fold_in(_tk, 500 + 25), (1250, 128), jnp.float32)
        _rk = jax.random.fold_in(_tk, 7)
        r_dense_features = -0.000520686 + 1.00062 * jax.random.normal(jax.random.fold_in(_rk, 101), (512, 128), jnp.float32)
        W_top1 = 0.0405887 * jax.random.normal(jax.random.fold_in(_tk, 801), (607, 512), jnp.float32)
        W_top2 = 0.0441942 * jax.random.normal(jax.random.fold_in(_tk, 802), (512, 256), jnp.float32)
        W_top3 = 0.0625 * jax.random.normal(jax.random.fold_in(_tk, 803), (256, 1), jnp.float32)
        b_top1 = jnp.zeros((512,), jnp.float32)
        b_top2 = jnp.zeros((256,), jnp.float32)
        return (r_dense_features, ids, tbl_0, tbl_1, tbl_2, tbl_3, tbl_4, tbl_5, tbl_6, tbl_7, tbl_8, tbl_9, tbl_10, tbl_11, tbl_12, tbl_13, tbl_14, tbl_15, tbl_16, tbl_17, tbl_18, tbl_19, tbl_20, tbl_21, tbl_22, tbl_23, tbl_24, tbl_25, W_top1, b_top1, W_top2, b_top2, W_top3)
    r_dense_features, ids, tbl_0, tbl_1, tbl_2, tbl_3, tbl_4, tbl_5, tbl_6, tbl_7, tbl_8, tbl_9, tbl_10, tbl_11, tbl_12, tbl_13, tbl_14, tbl_15, tbl_16, tbl_17, tbl_18, tbl_19, tbl_20, tbl_21, tbl_22, tbl_23, tbl_24, tbl_25, W_top1, b_top1, W_top2, b_top2, W_top3 = _rec_inputs()

    def _L0_rec_setup():
        import jax, jax.numpy as jnp
        import numpy as np
        F = 26
        N = F + 1
        _TRIU_I, _TRIU_J = np.triu_indices(N, k=1)
        key = jax.random.key(seed)
        k1, k2 = jax.random.split(key)
        B, D = (2048, 128)
        dense_features = jax.random.normal(k1, (B, D), dtype=jnp.float32)
        sparse_features = jax.random.normal(k2, (B, F, D), dtype=jnp.float32)
        return {'dense_features': dense_features, 'sparse_features': sparse_features}
    _L0_rec_all = _L0_rec_setup()
    _L0_rec_in = {k: v for k, v in _L0_rec_all.items() if k in ()}
    del _L0_rec_all
    return {'r_dense_features': r_dense_features, 'ids': ids, 'tbl_0': tbl_0, 'tbl_1': tbl_1, 'tbl_2': tbl_2, 'tbl_3': tbl_3, 'tbl_4': tbl_4, 'tbl_5': tbl_5, 'tbl_6': tbl_6, 'tbl_7': tbl_7, 'tbl_8': tbl_8, 'tbl_9': tbl_9, 'tbl_10': tbl_10, 'tbl_11': tbl_11, 'tbl_12': tbl_12, 'tbl_13': tbl_13, 'tbl_14': tbl_14, 'tbl_15': tbl_15, 'tbl_16': tbl_16, 'tbl_17': tbl_17, 'tbl_18': tbl_18, 'tbl_19': tbl_19, 'tbl_20': tbl_20, 'tbl_21': tbl_21, 'tbl_22': tbl_22, 'tbl_23': tbl_23, 'tbl_24': tbl_24, 'tbl_25': tbl_25, 'W_top1': W_top1, 'b_top1': b_top1, 'W_top2': W_top2, 'b_top2': b_top2, 'W_top3': W_top3}

def reference(r_dense_features, ids, tbl_0, tbl_1, tbl_2, tbl_3, tbl_4, tbl_5, tbl_6, tbl_7, tbl_8, tbl_9, tbl_10, tbl_11, tbl_12, tbl_13, tbl_14, tbl_15, tbl_16, tbl_17, tbl_18, tbl_19, tbl_20, tbl_21, tbl_22, tbl_23, tbl_24, tbl_25, W_top1, b_top1, W_top2, b_top2, W_top3):
    import jax
    import jax.numpy as jnp

    def _L0_rec_ref(dense_features, sparse_features):
        import jax, jax.numpy as jnp
        import numpy as np
        F = 26
        N = F + 1
        _TRIU_I, _TRIU_J = np.triu_indices(N, k=1)
        combined = jnp.concatenate([dense_features[:, None, :], sparse_features], axis=1)
        interactions = jnp.einsum('bnd,bmd->bnm', combined, combined)
        interactions_flat = interactions[:, _TRIU_I, _TRIU_J]
        return jnp.concatenate([dense_features, interactions_flat], axis=1)
    e = jnp.stack([tbl_0[ids[:, 0]], tbl_1[ids[:, 1]], tbl_2[ids[:, 2]], tbl_3[ids[:, 3]], tbl_4[ids[:, 4]], tbl_5[ids[:, 5]], tbl_6[ids[:, 6]], tbl_7[ids[:, 7]], tbl_8[ids[:, 8]], tbl_9[ids[:, 9]], tbl_10[ids[:, 10]], tbl_11[ids[:, 11]], tbl_12[ids[:, 12]], tbl_13[ids[:, 13]], tbl_14[ids[:, 14]], tbl_15[ids[:, 15]], tbl_16[ids[:, 16]], tbl_17[ids[:, 17]], tbl_18[ids[:, 18]], tbl_19[ids[:, 19]], tbl_20[ids[:, 20]], tbl_21[ids[:, 21]], tbl_22[ids[:, 22]], tbl_23[ids[:, 23]], tbl_24[ids[:, 24]], tbl_25[ids[:, 25]]], axis=1)
    z = _L0_rec_ref(r_dense_features, e)
    z = z.reshape(z.shape[0], -1)
    h = jnp.concatenate([z, r_dense_features], axis=1)
    h = jnp.maximum(h @ W_top1 + b_top1, 0.0)
    h = jnp.maximum(h @ W_top2 + b_top2, 0.0)
    y = h @ W_top3
    return y

_drawn_inputs = setup_inputs


def setup_inputs(seed=0):
    import zlib

    import numpy as np

    out = dict(_drawn_inputs(seed))
    spreads = {'b_top1': (0.0, 0.1), 'b_top2': (0.0, 0.1)}
    factors = {}
    for name, (base, spread) in spreads.items():
        noise = np.random.default_rng([zlib.crc32(name.encode()), seed]).standard_normal(out[name].shape)
        drawn = base * np.exp(spread * noise) if base else spread * noise
        out[name] = jnp.asarray(drawn.astype(out[name].dtype))
    for name, factor in factors.items():
        out[name] = (out[name] * factor).astype(out[name].dtype)
    return out
```

```python
from contextlib import ExitStack

import numpy as np
import concourse.bass as bass
from concourse import mybir

P = 128
BATCH = 512
D = 128
TABLES = 26
ROWS = [1000, 125000, 1250, 12500, 1000, 1250, 1250, 12500, 1000, 1000, 1000, 1000, 1250,
        1000, 1000, 12500, 12500, 1250, 1000, 1250, 1250, 12500, 1250, 12500, 1000, 1250]
FEATURES = TABLES + 1
HIDDEN1, HIDDEN2 = 512, 256

SHORT = min(ROWS)
ONE_HOT = [f for f in range(TABLES) if ROWS[f] == SHORT][:9]
GATHERED = [f for f in range(TABLES) if f not in ONE_HOT]
ROW_PARTS = 125
CHUNKS = SHORT // ROW_PARTS
NQ, NG = len(ONE_HOT), len(GATHERED)

TILE = P
TILES = BATCH // TILE
SLOTS = FEATURES + 1
ZERO_SLOT = FEATURES
FEATURE_OF_SLOT = [0] + [f + 1 for f in ONE_HOT] + [f + 1 for f in GATHERED]

SAMPLES_AT_ONCE = 4
QUADRANT = P // SAMPLES_AT_ONCE
GROUPS = TILE // SAMPLES_AT_ONCE
HALF_GROUPS = GROUPS // 2
JLOW = 4
JQ = SLOTS // JLOW
STEPS = [(0, 3, 11, 0), (3, 2, 19, 33), (5, 2, 27, 71)]
PAIR_ROWS = 125

GATHERS_PER_BANK = 4
GATHER_LOTS = [list(range(k, min(k + GATHERS_PER_BANK, NG))) for k in range(0, NG, GATHERS_PER_BANK)]
LOTS = len(GATHER_LOTS)

RAW_RING, SPLIT_RING, ONE_HOT_RING, IDS_RING = 3, 2, 2, 3

C_IDENT, C_ROW, C_B1, C_B2, C_W3 = 0, P, P + CHUNKS, P + CHUNKS + 4, P + CHUNKS + 6
C_END = C_W3 + 2


def pair_rows():
    rows = np.full((PAIR_ROWS, JLOW), -1)
    for jq0, count, kept, first in STEPS:
        for jq in range(jq0, jq0 + count):
            for jj in range(JLOW):
                j = JLOW * jq + jj
                for i in range(min(kept, j) if j < FEATURES else 0):
                    a, b = sorted((FEATURE_OF_SLOT[i], FEATURE_OF_SLOT[j]))
                    rows[first + (jq - jq0) * kept + i, jj] = (
                        D + a * (FEATURES - 1) - a * (a - 1) // 2 + b - a - 1)
    return rows


def fill_order():
    early = [("gather", t, l) for t in range(2) for l in range(LOTS)]
    fills = []
    for q in range(NQ):
        fills.append(("one_hot", q, "act"))
        if q >= 2 and len(early) > LOTS:
            fills.append((*early.pop(0), "act"))
    fills += [(*e, "act") for e in early if e[1] == 0]
    for t in range(1, TILES):
        fills += [("gather", t, l, "act" if l % 2 else "dve") for l in range(LOTS)]
    return fills


FILLS = fill_order()


def copies_until(engine, last):
    return sum(f[-1] == engine for f in FILLS[:last + 1])


def last_fill_of(tile):
    return max(k for k, f in enumerate(FILLS) if f[0] == "one_hot" or f[1] == tile)


def dlrm_tower(nc, ids_gather, ids_one_hot, dense_t, tables, w_pairs, w_dense, w2, small, out):
    f32, f32r, i32 = mybir.dt.float32, mybir.dt.float32r, mybir.dt.int32
    ALU = mybir.AluOpType
    ACT = mybir.ActivationFunctionType

    with ExitStack() as ctx:
        def sb(name, shape, dtype=f32):
            return ctx.enter_context(nc.sbuf_tensor(name, shape, dtype))

        def bank(name):
            return ctx.enter_context(nc.psum_tensor(name, [P, 512], f32))

        def sem(name):
            return ctx.enter_context(nc.semaphore(name))

        gather_ids = sb("gather_ids", [P, TILES * NG], i32)
        gathered = sb("gathered", [P, TILES, NG, D])
        spread_ids = sb("spread_ids", [P, IDS_RING, BATCH], i32)
        table_raw = sb("table_raw", [P, RAW_RING, CHUNKS, D])
        table_hi = sb("table_hi", [P, SPLIT_RING, CHUNKS, D], f32r)
        table_lo = sb("table_lo", [P, SPLIT_RING, CHUNKS, D], f32r)
        one_hot = sb("one_hot", [P, ONE_HOT_RING, CHUNKS, BATCH], f32r)
        dense = sb("dense", [P, BATCH])
        columns = sb("columns", [P, BATCH, SLOTS])
        gram = sb("gram", [P, SLOTS, GROUPS])
        half_turned = sb("half_turned", [P, SAMPLES_AT_ONCE, PAIR_ROWS])
        pairs = sb("pairs", [PAIR_ROWS, JLOW, TILE])
        w_pairs_sb = sb("w_pairs_sb", [PAIR_ROWS, JLOW, HIDDEN1])
        w_dense_parts = sb("w_dense_parts", [P, 2, HIDDEN1])
        w_dense_sum = sb("w_dense_sum", [P, HIDDEN1])
        w2_sb = sb("w2_sb", [P, HIDDEN1 // P, HIDDEN2])
        hidden1 = sb("hidden1", [P, HIDDEN1 // P, TILE])
        hidden2 = sb("hidden2", [P, HIDDEN2 // P, TILE])
        consts = sb("consts", [P, C_END])
        y = sb("y", [1, BATCH])
        ident = consts[:, C_IDENT:C_IDENT + P]

        fill_bank = [bank("fill_bank0"), bank("fill_bank1")]
        gram_bank = [bank("gram_bank0"), bank("gram_bank1")]
        turn_bank = [bank("turn_bank0"), bank("turn_bank1")]
        pairs_bank = bank("pairs_bank")
        layer_bank = bank("layer_bank")

        gather_ids_in = sem("gather_ids_in")
        consts_in = sem("consts_in")
        dense_in = sem("dense_in")
        spread_ids_in = [sem(f"spread_ids_in{r}") for r in range(IDS_RING)]
        table_in = [sem(f"table_in{r}") for r in range(RAW_RING)]
        rows_in = [[sem(f"rows_in{t}_{l}") for l in range(LOTS)] for t in range(TILES)]
        w_pairs_in = sem("w_pairs_in")
        w_dense_in = sem("w_dense_in")
        w2_in = sem("w2_in")
        hi_ready = sem("hi_ready")
        lo_ready = sem("lo_ready")
        one_hot_ready = sem("one_hot_ready")
        table_done = sem("table_done")
        fill_done = sem("fill_done")
        copied = {"act": sem("copied_by_act"), "dve": sem("copied_by_dve")}
        dense_slot_ready = sem("dense_slot_ready")
        zero_slot_ready = sem("zero_slot_ready")
        gram_pads_ready = sem("gram_pads_ready")
        gram_done = sem("gram_done")
        gram_copied = [sem("gram_copied0"), sem("gram_copied1")]
        turn_done = [sem("turn_done0"), sem("turn_done1")]
        turn_copied = [sem("turn_copied0"), sem("turn_copied1")]
        pairs_done = sem("pairs_done")
        pairs_copied = sem("pairs_copied")
        w_dense_ready = sem("w_dense_ready")
        layer1_done = sem("layer1_done")
        hidden1_ready = sem("hidden1_ready")
        layer2_done = sem("layer2_done")
        hidden2_ready = sem("hidden2_ready")
        layer3_done = sem("layer3_done")
        y_ready = sem("y_ready")
        out_written = sem("out_written")

        block = ctx.enter_context(nc.Block())

        @block.sync
        def _(sp):
            sp.dma_start(gather_ids[:], ids_gather).then_inc(gather_ids_in, 16)

            def load_table(q):
                table = tables[ONE_HOT[q]].rearrange("(p c) d -> p (c d)", c=CHUNKS)
                even = ROW_PARTS // 16 * 16
                dst = table_raw[:, q % RAW_RING].rearrange("p c d -> p (c d)")
                if q >= RAW_RING:
                    sp.wait_ge(lo_ready, q - RAW_RING + 1)
                sp.dma_start(dst[0:even, :], table[0:even, :]).then_inc(table_in[q % RAW_RING], 16)
                sp.dma_start(dst[even:ROW_PARTS, :],
                             table[even:ROW_PARTS, :]).then_inc(table_in[q % RAW_RING], 16)

            for q in range(NQ):
                load_table(q)
                if q == 2:
                    sp.dma_start(w_pairs_sb[:], w_pairs).then_inc(w_pairs_in, 16)
                if q == 3:
                    sp.dma_start(w_dense_parts[:], w_dense).then_inc(w_dense_in, 16)
                    sp.dma_start(w2_sb[:], w2).then_inc(w2_in, 16)
            sp.wait_ge(y_ready, TILES)
            sp.dma_start(out, y[:]).then_inc(out_written, 16)
            sp.wait_ge(out_written, 16)

        @block.gpsimd
        def _(pool):
            pool.wait_ge(gather_ids_in, 16)
            for t in range(TILES):
                for lot, members in enumerate(GATHER_LOTS):
                    for k in members:
                        at = t * NG + k
                        pool.indirect_dma_start(
                            out=gathered[:, t, k, :], out_offset=None, in_=tables[GATHERED[k]],
                            in_offset=bass.IndirectOffsetOnAxis(ap=gather_ids[:, at:at + 1], axis=0),
                        ).then_inc(rows_in[t][lot], 16)

        def copy_fill(engine, copy, k):
            fill = FILLS[k]
            engine.wait_ge(fill_done, k + 1)
            if fill[0] == "one_hot":
                src = fill_bank[k % 2][:, :]
                dst = columns[:, :, 1 + fill[1]]
            else:
                members = GATHER_LOTS[fill[2]]
                slot = 1 + NQ + members[0]
                n0 = fill[1] * TILE
                src = fill_bank[k % 2][:, 0:len(members) * TILE].rearrange("p (f n) -> p n f", n=TILE)
                dst = columns[:, n0:n0 + TILE, slot:slot + len(members)]
            copy(dst, src).then_inc(copied[fill[-1]], 1)

        def copy_fills(engine, copy, who, first, end):
            for k in range(first, end):
                if FILLS[k][-1] == who:
                    copy_fill(engine, copy, k)

        def gram_halves(half):
            src = gram_bank[half][:, 0:HALF_GROUPS * SLOTS].rearrange("p (g j) -> p j g", j=SLOTS)
            return gram[:, :, half * HALF_GROUPS:(half + 1) * HALF_GROUPS], src

        def turned(step):
            jq0, count, kept, first = STEPS[step]
            at = jq0 if step == 0 else jq0 - STEPS[1][0]
            src = turn_bank[min(step, 1)][:, at * P:(at + count) * P].rearrange(
                "p (q s i) -> p q s i", q=count, i=QUADRANT)[:, :, :, 0:kept]
            dst = half_turned[:, :, first:first + count * kept].rearrange("p s (q i) -> p q s i", q=count)
            return dst, src

        whole = [last_fill_of(t) for t in range(TILES)]

        @block.scalar
        def _(act):
            copy = nc.scalar.copy
            act.dma_start(consts[:], small).then_inc(consts_in, 16)
            for q in range(IDS_RING):
                act.dma_start(spread_ids[:, q, :],
                              ids_one_hot[q:q + 1, :].partition_broadcast(P)).then_inc(spread_ids_in[q], 16)
                if q == 0:
                    act.dma_start(dense[:], dense_t).then_inc(dense_in, 16)

            def split_hi(q):
                act.wait_ge(table_in[q % RAW_RING], 32 * (q // RAW_RING + 1))
                if q >= SPLIT_RING:
                    act.wait_ge(table_done, q - SPLIT_RING + 1)
                copy(table_hi[0:ROW_PARTS, q % SPLIT_RING],
                     table_raw[0:ROW_PARTS, q % RAW_RING]).then_inc(hi_ready, 1)

            split_hi(0)
            split_hi(1)
            act.wait_ge(dense_in, 16)
            copy(columns[:, :, 0], dense[:]).then_inc(dense_slot_ready, 1)
            done = 0
            for k, fill in enumerate(FILLS[:whole[0] + 1]):
                if fill[0] == "one_hot":
                    q = fill[1]
                    if q + 2 < NQ:
                        split_hi(q + 2)
                    if q + IDS_RING < NQ:
                        act.wait_ge(one_hot_ready, (q + 1) * CHUNKS)
                        act.dma_start(spread_ids[:, q % IDS_RING, :],
                                      ids_one_hot[q + IDS_RING:q + IDS_RING + 1, :].partition_broadcast(P)
                                      ).then_inc(spread_ids_in[q % IDS_RING], 16)
                copy_fill(act, copy, k)

            def to_pairs(t):
                act.wait_ge(gram_done, 2 * t + 1)
                copy(*gram_halves(0)).then_inc(gram_copied[0], 1)

            def turn(t):
                act.wait_ge(turn_done[0], t + 1)
                copy(*turned(0)).then_inc(turn_copied[0], 1)

            def layer1(t):
                act.wait_ge(layer1_done, t + 1)
                for m in range(HIDDEN1 // P):
                    last = nc.scalar.activation(
                        hidden1[:, m, :], layer_bank[:, m * TILE:(m + 1) * TILE], ACT.Relu,
                        bias=consts[:, C_B1 + m:C_B1 + m + 1])
                last.then_inc(hidden1_ready, 1)

            def layer2(t):
                act.wait_ge(layer2_done, t + 1)
                for m in range(HIDDEN2 // P):
                    last = nc.scalar.activation(
                        hidden2[:, m, :], layer_bank[:, m * TILE:(m + 1) * TILE], ACT.Relu,
                        bias=consts[:, C_B2 + m:C_B2 + m + 1])
                last.then_inc(hidden2_ready, 1)

            def layer3(t):
                act.wait_ge(layer3_done, t + 1)
                copy(y[0:1, t * TILE:(t + 1) * TILE], layer_bank[0:1, 0:TILE]).then_inc(y_ready, 1)

            act.wait_ge(consts_in, 16)
            for t in range(TILES):
                ahead = t - 1 if 0 < t < TILES - 1 else None
                to_pairs(t)
                if ahead is not None:
                    layer1(ahead)
                turn(t)
                if ahead is not None:
                    layer2(ahead)
                    layer3(ahead)
                if t == TILES - 2:
                    layer1(t)
                    layer2(t)
                    layer3(t)
                if t + 1 < TILES:
                    copy_fills(act, copy, "act", whole[t] + 1, whole[t + 1] + 1)
            layer1(TILES - 1)
            layer2(TILES - 1)
            layer3(TILES - 1)

        @block.vector
        def _(dve):
            copy = nc.vector.tensor_copy
            nc.vector.memset(columns[:, :, ZERO_SLOT], 0.0).then_inc(zero_slot_ready, 1)
            for half in range(2):
                nc.vector.memset(gram_bank[half][:], 0.0).then_inc(gram_pads_ready, 1)
            dve.wait_ge(consts_in, 16)
            for q in range(NQ):
                dve.wait_ge(spread_ids_in[q % IDS_RING], 16 * (q // IDS_RING + 1))
                if q >= ONE_HOT_RING:
                    dve.wait_ge(table_done, q - ONE_HOT_RING + 1)
                for c in range(CHUNKS):
                    nc.vector.tensor_scalar(
                        one_hot[0:ROW_PARTS, q % ONE_HOT_RING, c, :],
                        spread_ids[0:ROW_PARTS, q % IDS_RING, :],
                        consts[0:ROW_PARTS, C_ROW + c:C_ROW + c + 1], None,
                        ALU.is_equal).then_inc(one_hot_ready, 1)
                dve.wait_ge(hi_ready, q + 1)
                nc.vector.tensor_tensor(
                    table_lo[0:ROW_PARTS, q % SPLIT_RING], table_raw[0:ROW_PARTS, q % RAW_RING],
                    table_hi[0:ROW_PARTS, q % SPLIT_RING].bitcast(f32), ALU.subtract).then_inc(lo_ready, 1)
            dve.wait_ge(w_dense_in, 16)
            nc.vector.tensor_tensor(w_dense_sum[:], w_dense_parts[:, 0, :], w_dense_parts[:, 1, :],
                                    ALU.add).then_inc(w_dense_ready, 1)
            for t in range(TILES):
                dve.wait_ge(gram_done, 2 * t + 2)
                copy(*gram_halves(1)).then_inc(gram_copied[1], 1)
                dve.wait_ge(turn_done[1], t + 1)
                copy(*turned(1))
                copy(*turned(2)).then_inc(turn_copied[1], 1)
                dve.wait_ge(pairs_done, t + 1)
                copy(pairs[:].rearrange("c j (s g) -> c s j g", g=GROUPS),
                     pairs_bank[0:PAIR_ROWS, :].rearrange("c (s j g) -> c s j g", s=SAMPLES_AT_ONCE, g=GROUPS)
                     ).then_inc(pairs_copied, 1)
                if t + 1 < TILES:
                    copy_fills(dve, copy, "dve", whole[t] + 1, whole[t + 1] + 1)

        @block.tensor
        def _(pe):
            def bank_free(k):
                if k >= 2:
                    who = FILLS[k - 2][-1]
                    pe.wait_ge(copied[who], copies_until(who, k - 2))

            def fill(k):
                kind = FILLS[k]
                bank_free(k)
                if kind[0] == "one_hot":
                    q = kind[1]
                    pe.wait_ge(hi_ready, q + 1)
                    for c in range(CHUNKS):
                        pe.wait_ge(one_hot_ready, q * CHUNKS + c + 1)
                        nc.tensor.matmul(fill_bank[k % 2][:], table_hi[0:ROW_PARTS, q % SPLIT_RING, c, :],
                                         one_hot[0:ROW_PARTS, q % ONE_HOT_RING, c, :],
                                         start=(c == 0), stop=False)
                    pe.wait_ge(lo_ready, q + 1)
                    for c in range(CHUNKS):
                        last = nc.tensor.matmul(fill_bank[k % 2][:], table_lo[0:ROW_PARTS, q % SPLIT_RING, c, :],
                                                one_hot[0:ROW_PARTS, q % ONE_HOT_RING, c, :],
                                                start=False, stop=(c == CHUNKS - 1))
                    last.then_inc(fill_done, 1)
                    pe.wait_ge(fill_done, k + 1)
                    pe.sem_inc(table_done, 1)
                else:
                    t, lot = kind[1], kind[2]
                    members = GATHER_LOTS[lot]
                    pe.wait_ge(rows_in[t][lot], 16 * len(members))
                    for n, f in enumerate(members):
                        last = nc.tensor.transpose(fill_bank[k % 2][:, n * TILE:(n + 1) * TILE],
                                                   gathered[:, t, f, :], ident)
                    last.then_inc(fill_done, 1)

            def dot_products(t):
                for who in ("act", "dve"):
                    if copies_until(who, whole[t]):
                        pe.wait_ge(copied[who], copies_until(who, whole[t]))
                for half in range(2):
                    if t:
                        pe.wait_ge(gram_copied[half], t)
                    for g in range(HALF_GROUPS):
                        for s in range(SAMPLES_AT_ONCE):
                            n = t * TILE + s * GROUPS + half * HALF_GROUPS + g
                            last = nc.tensor.matmul(
                                gram_bank[half][s * QUADRANT:s * QUADRANT + SLOTS, g * SLOTS:(g + 1) * SLOTS],
                                columns[:, n, :], columns[:, n, :], start=True, stop=True)
                    last.then_inc(gram_done, 1)

            def first_turn(t):
                for half in range(2):
                    pe.wait_ge(gram_copied[half], t + 1)
                for b, (jq0, jq1) in enumerate(((0, STEPS[1][0]), (STEPS[1][0], JQ))):
                    if t:
                        pe.wait_ge(turn_copied[b], t)
                    for jq in range(jq0, jq1):
                        last = nc.tensor.transpose(
                            turn_bank[b][:, (jq - jq0) * P:(jq - jq0 + 1) * P],
                            gram[:, JLOW * jq:JLOW * (jq + 1), :].rearrange("p j g -> p (j g)"), ident)
                    last.then_inc(turn_done[b], 1)

            def second_turn(t):
                for b in range(2):
                    pe.wait_ge(turn_copied[b], t + 1)
                if t:
                    pe.wait_ge(pairs_copied, t)
                for s in range(SAMPLES_AT_ONCE):
                    last = nc.tensor.transpose(pairs_bank[0:PAIR_ROWS, s * P:(s + 1) * P],
                                               half_turned[:, s, :], ident)
                last.then_inc(pairs_done, 1)

            def layer1(t):
                if t == 0:
                    pe.wait_ge(w_dense_ready, 1)
                    pe.wait_ge(w_pairs_in, 16)
                else:
                    pe.wait_ge(y_ready, t)
                pe.wait_ge(pairs_copied, t + 1)
                for m in range(HIDDEN1 // P):
                    o = layer_bank[:, m * TILE:(m + 1) * TILE]
                    units = slice(m * P, (m + 1) * P)
                    nc.tensor.matmul(o, w_dense_sum[:, units], dense[:, t * TILE:(t + 1) * TILE],
                                     start=True, stop=False)
                    for jj in range(JLOW):
                        last = nc.tensor.matmul(o, w_pairs_sb[:, jj, units], pairs[:, jj, :],
                                                start=False, stop=(jj == JLOW - 1))
                last.then_inc(layer1_done, 1)

            def layer2(t):
                if t == 0:
                    pe.wait_ge(w2_in, 16)
                pe.wait_ge(hidden1_ready, t + 1)
                for m in range(HIDDEN2 // P):
                    for k in range(HIDDEN1 // P):
                        last = nc.tensor.matmul(layer_bank[:, m * TILE:(m + 1) * TILE],
                                                w2_sb[:, k, m * P:(m + 1) * P], hidden1[:, k, :],
                                                start=(k == 0), stop=(k == HIDDEN1 // P - 1))
                last.then_inc(layer2_done, 1)

            def layer3(t):
                pe.wait_ge(hidden2_ready, t + 1)
                for k in range(HIDDEN2 // P):
                    last = nc.tensor.matmul(layer_bank[0:1, 0:TILE], consts[:, C_W3 + k:C_W3 + k + 1],
                                            hidden2[:, k, :], start=(k == 0), stop=(k == HIDDEN2 // P - 1))
                last.then_inc(layer3_done, 1)

            pe.wait_ge(consts_in, 16)
            for k in range(whole[0] + 1):
                fill(k)
            pe.wait_ge(dense_slot_ready, 1)
            pe.wait_ge(zero_slot_ready, 1)
            pe.wait_ge(gram_pads_ready, 2)
            for t in range(TILES):
                between = 0 < t < TILES - 1
                dot_products(t)
                if between:
                    layer1(t - 1)
                first_turn(t)
                if between:
                    layer2(t - 1)
                second_turn(t)
                if between:
                    layer3(t - 1)
                if t == TILES - 2:
                    layer1(t)
                    layer2(t)
                    layer3(t)
                if t + 1 < TILES:
                    for k in range(whole[t] + 1, whole[t + 1] + 1):
                        fill(k)
            layer1(TILES - 1)
            layer2(TILES - 1)
            layer3(TILES - 1)


def kernel(**inputs):
    import concourse.bacc as bacc
    from concourse.bass_utils import run_bass_kernel_spmd

    x = {name: np.ascontiguousarray(a) for name, a in inputs.items()}
    ids = x["ids"]
    w1 = x["W_top1"]
    padded = np.concatenate([w1, np.zeros((1, HIDDEN1), w1.dtype)])
    by_chunk = np.arange(ROW_PARTS)[:, None] * CHUNKS + np.arange(CHUNKS)
    small = np.zeros((P, C_END), np.float32)
    small[:, C_IDENT:C_IDENT + P] = np.eye(P, dtype=np.float32)
    small[0:ROW_PARTS, C_ROW:C_ROW + CHUNKS] = by_chunk
    small[:, C_B1:C_B2] = x["b_top1"].reshape(-1, P).T
    small[:, C_B2:C_W3] = x["b_top2"].reshape(-1, P).T
    small[:, C_W3:C_END] = x["W_top3"].reshape(-1, P).T
    arrays = {
        "ids_gather": ids[:, GATHERED].reshape(TILES, TILE, NG).transpose(1, 0, 2).reshape(P, TILES * NG),
        "ids_one_hot": ids[:, ONE_HOT].T,
        "dense_t": x["r_dense_features"].T,
        "w_pairs": padded[pair_rows()],
        "w_dense": np.stack([w1[0:D], w1[-D:]], axis=1),
        "w2": x["W_top2"].reshape(HIDDEN1 // P, P, HIDDEN2).transpose(1, 0, 2),
        "small": small,
    }
    arrays |= {f"tbl_{f}": x[f"tbl_{f}"] for f in range(TABLES)}
    arrays = {name: np.ascontiguousarray(a) for name, a in arrays.items()}

    nc = bacc.Bacc("TRN2", target_bir_lowering=False, num_devices=1)
    d = {name: nc.dram_tensor(name, a.shape, mybir.dt.from_np(a.dtype), kind="ExternalInput").ap()
         for name, a in arrays.items()}
    out = nc.dram_tensor("out", (BATCH, 1), mybir.dt.float32, kind="ExternalOutput").ap()
    dlrm_tower(nc, d["ids_gather"], d["ids_one_hot"], d["dense_t"],
               [d[f"tbl_{f}"] for f in range(TABLES)], d["w_pairs"], d["w_dense"], d["w2"], d["small"],
               out.rearrange("b one -> one b"))
    r = run_bass_kernel_spmd(nc, [arrays], core_ids=[0])
    return r.results[0]["out"]
```

```python
from contextlib import ExitStack

import numpy as np
import concourse.bass as bass
from concourse import mybir

P = 128
BATCH = 512
D = 128
TABLES = 26
ROWS = [1000, 125000, 1250, 12500, 1000, 1250, 1250, 12500, 1000, 1000, 1000, 1000, 1250,
        1000, 1000, 12500, 12500, 1250, 1000, 1250, 1250, 12500, 1250, 12500, 1000, 1250]
FEATURES = TABLES + 1
HIDDEN1, HIDDEN2 = 512, 256
UNIT_BLOCKS1, UNIT_BLOCKS2 = HIDDEN1 // P, HIDDEN2 // P
HALF_BLOCKS1 = UNIT_BLOCKS1 // 2

SHORT = min(ROWS)
ONE_HOT = [f for f in range(TABLES) if ROWS[f] == SHORT][:9]
GATHERED = [f for f in range(TABLES) if f not in ONE_HOT]
ROW_PARTS = 125
CHUNKS = SHORT // ROW_PARTS
NQ, NG = len(ONE_HOT), len(GATHERED)

TILE = P
TILES = BATCH // TILE
SLOTS = FEATURES
FEATURE_OF_SLOT = [0] + [f + 1 for f in ONE_HOT] + [f + 1 for f in GATHERED]

SAMPLES_AT_ONCE = 4
QUADRANT = P // SAMPLES_AT_ONCE
GROUPS = TILE // SAMPLES_AT_ONCE
HALF_GROUPS = GROUPS // 2
JLOW = 3
JQ = SLOTS // JLOW
TURNED = JLOW * GROUPS
KEPT = [JLOW * (jq + 1) - 1 for jq in range(JQ)]
PAIR_AT = [sum(KEPT[:jq]) for jq in range(JQ)]
PAIR_ROWS = sum(KEPT)
BLOCKS_PER_BANK = 4
TURN_LOTS = [range(b, min(b + BLOCKS_PER_BANK, JQ)) for b in range(0, JQ, BLOCKS_PER_BANK)]

GATHERS_PER_BANK = 4
GATHER_LOTS = [list(range(k, min(k + GATHERS_PER_BANK, NG))) for k in range(0, NG, GATHERS_PER_BANK)]
LOTS = len(GATHER_LOTS)

WARM_PRODUCTS = 13
RAW_RING, SPLIT_RING, ONE_HOT_RING, IDS_RING = 3, 2, 2, 3

C_IDENT, C_BASE, C_B1, C_B2, C_W3 = 0, P, P + 1, P + 5, P + 7
C_END = C_W3 + 2


def pair_rows():
    rows = np.full((PAIR_ROWS, JLOW), -1)
    for jq in range(JQ):
        for jj in range(JLOW):
            j = JLOW * jq + jj
            for i in range(j):
                a, b = sorted((FEATURE_OF_SLOT[i], FEATURE_OF_SLOT[j]))
                rows[PAIR_AT[jq] + i, jj] = D + a * (FEATURES - 1) - a * (a - 1) // 2 + b - a - 1
    return rows


def stages():
    def fills(t, lots):
        return [("gather", t, lot) for lot in lots]

    lots = range(LOTS)
    order = []
    early = fills(0, lots)
    for q in range(NQ):
        order.append(("one_hot", q))
        if q >= 1 and early:
            order.append(early.pop(0))
    order += early + fills(1, lots[:2])
    order += [("gram", 0, 0), ("gram", 0, 1), *fills(1, lots[2:4]), ("first_turn", 0),
              *fills(1, lots[4:]), *fills(2, lots[:1]), ("second_turn", 0),
              ("gram", 1, 0), ("layer1", 0, 0), ("gram", 1, 1), ("layer1", 0, 1), ("first_turn", 1),
              *fills(2, lots[1:3]), ("second_turn", 1), ("layer2", 0, 0), *fills(2, lots[3:]), ("layer2", 0, 1),
              ("gram", 2, 0), ("layer3", 0), ("layer1", 1, 0), ("gram", 2, 1), ("layer1", 1, 1), ("first_turn", 2),
              *fills(3, lots[:2]), ("second_turn", 2), ("layer2", 1, 0), *fills(3, lots[2:3]), ("layer2", 1, 1),
              ("layer1", 2, 0), *fills(3, lots[3:4]), ("layer3", 1), *fills(3, lots[4:]), ("layer1", 2, 1),
              ("gram", 3, 0), ("gram", 3, 1), ("layer2", 2, 0), ("first_turn", 3), ("layer2", 2, 1),
              ("second_turn", 3), ("layer3", 2), ("layer1", 3, 0), ("layer1", 3, 1), ("layer2", 3, 0),
              ("layer2", 3, 1), ("layer3", 3)]
    return order


STAGES = stages()
FILLS = [s for s in STAGES if s[0] in ("one_hot", "gather")]
ONE_HOT_DONE = STAGES.index(("one_hot", NQ - 1))


EARLY_FILLS = sum(s[0] in ("one_hot", "gather") for s in STAGES[:STAGES.index(("gram", 0, 0))])


def fills_with(q):
    return FILLS.index(("one_hot", q)) + 1


def copier(k):
    late = STAGES.index(FILLS[k]) > ONE_HOT_DONE
    return "dve" if late and k % 2 else "act"


def copies_until(engine, last):
    return sum(copier(k) == engine for k in range(last + 1))


def bank_of(k):
    return k % 4 if k < EARLY_FILLS else (k - EARLY_FILLS) % 2


def before_in_bank(k):
    return max((n for n in range(k) if bank_of(n) == bank_of(k)), default=None)


def last_fill_of(tile):
    return max(k for k, f in enumerate(FILLS) if f[0] == "one_hot" or f[1] == tile)


def dlrm_tower(nc, ids_gather, ids_one_hot, dense_t, tables, w_pairs, w_dense, w2, small, out):
    f32, f32r, i32 = mybir.dt.float32, mybir.dt.float32r, mybir.dt.int32
    ALU = mybir.AluOpType
    ACT = mybir.ActivationFunctionType

    with ExitStack() as ctx:
        def sb(name, shape, dtype=f32):
            return ctx.enter_context(nc.sbuf_tensor(name, shape, dtype))

        def bank(name):
            return ctx.enter_context(nc.psum_tensor(name, [P, 512], f32))

        def sem(name):
            return ctx.enter_context(nc.semaphore(name))

        gather_ids = sb("gather_ids", [P, TILES * NG], i32)
        gathered = sb("gathered", [P, TILES, NG, D])
        spread_ids = sb("spread_ids", [P, IDS_RING, BATCH], i32)
        shifted_ids = sb("shifted_ids", [P, SPLIT_RING, BATCH])
        table_raw = sb("table_raw", [P, RAW_RING, CHUNKS, D])
        table_hi = sb("table_hi", [P, SPLIT_RING, CHUNKS, D], f32r)
        table_lo = sb("table_lo", [P, SPLIT_RING, CHUNKS, D], f32r)
        one_hot = sb("one_hot", [P, ONE_HOT_RING, CHUNKS, BATCH], f32r)
        dense = sb("dense", [P, BATCH])
        columns = sb("columns", [P, BATCH, SLOTS])
        gram = sb("gram", [P, SLOTS, GROUPS])
        half_turned = sb("half_turned", [TURNED, SAMPLES_AT_ONCE, PAIR_ROWS])
        pairs = sb("pairs", [PAIR_ROWS, JLOW, TILE])
        w_pairs_sb = sb("w_pairs_sb", [PAIR_ROWS, JLOW, HIDDEN1])
        w_dense_parts = sb("w_dense_parts", [P, 2, HIDDEN1])
        w_dense_sum = sb("w_dense_sum", [P, HIDDEN1])
        w2_sb = sb("w2_sb", [P, UNIT_BLOCKS1, HIDDEN2])
        hidden1 = sb("hidden1", [P, UNIT_BLOCKS1, TILE])
        hidden2 = sb("hidden2", [P, UNIT_BLOCKS2, TILE])
        consts = sb("consts", [P, C_END])
        warm = sb("warm", [P, BATCH], mybir.dt.bfloat16)
        warm_out = sb("warm_out", [P, 1])
        y = sb("y", [P, TILES])
        ident = consts[:, C_IDENT:C_IDENT + P]

        fill_bank = [bank(f"fill_bank{b}") for b in range(4)]
        gram_bank = [bank("gram_bank0"), bank("gram_bank1")]
        turn_bank = [fill_bank[2], fill_bank[3], gram_bank[0]]
        pairs_bank = bank("pairs_bank")
        layer_bank = bank("layer_bank")
        layer1_bank = [turn_bank[0], layer_bank]
        layer2_bank = [[gram_bank[1], turn_bank[1]] if t < TILES - 2 else fill_bank[0:2] for t in range(TILES)]

        gather_ids_in = sem("gather_ids_in")
        consts_in = sem("consts_in")
        dense_in = sem("dense_in")
        spread_ids_in = [sem(f"spread_ids_in{r}") for r in range(IDS_RING)]
        table_in = [sem(f"table_in{r}") for r in range(RAW_RING)]
        rows_in = [[sem(f"rows_in{t}_{lot}") for lot in range(LOTS)] for t in range(TILES)]
        w_pairs_in = sem("w_pairs_in")
        w_dense_in = sem("w_dense_in")
        w2_in = sem("w2_in")
        warm_ready = sem("warm_ready")
        shifted_ready = sem("shifted_ready")
        hi_ready = sem("hi_ready")
        lo_ready = sem("lo_ready")
        one_hot_ready = sem("one_hot_ready")
        fill_done = sem("fill_done")
        copied = {"act": sem("copied_by_act"), "dve": sem("copied_by_dve")}
        dense_slot_ready = sem("dense_slot_ready")
        gram_pads_ready = sem("gram_pads_ready")
        gram_done = sem("gram_done")
        gram_copied = [sem("gram_copied0"), sem("gram_copied1")]
        turn_done = [sem(f"turn_done{b}") for b in range(len(TURN_LOTS))]
        turn_copied = [sem(f"turn_copied{b}") for b in range(len(TURN_LOTS))]
        pairs_done = sem("pairs_done")
        pairs_copied = sem("pairs_copied")
        w_dense_ready = sem("w_dense_ready")
        layer1_done = sem("layer1_done")
        hidden1_ready = [sem("hidden1_ready0"), sem("hidden1_ready1")]
        layer2_done = sem("layer2_done")
        hidden2_ready = [sem("hidden2_ready0"), sem("hidden2_ready1")]
        layer3_done = sem("layer3_done")
        y_ready = sem("y_ready")
        out_written = sem("out_written")

        block = ctx.enter_context(nc.Block())

        @block.sync
        def _(sp):
            def load_table(q):
                table = tables[ONE_HOT[q]].rearrange("(p c) d -> p (c d)", c=CHUNKS)
                even = ROW_PARTS // 16 * 16
                dst = table_raw[:, q % RAW_RING].rearrange("p c d -> p (c d)")
                if q >= RAW_RING:
                    sp.wait_ge(lo_ready, q - RAW_RING + 1)
                sp.dma_start(dst[0:even, :], table[0:even, :]).then_inc(table_in[q % RAW_RING], 16)
                sp.dma_start(dst[even:ROW_PARTS, :],
                             table[even:ROW_PARTS, :]).then_inc(table_in[q % RAW_RING], 16)

            def load_spread_ids(q):
                if q >= IDS_RING:
                    sp.wait_ge(shifted_ready, q - IDS_RING + 1)
                sp.dma_start(spread_ids[:, q % IDS_RING, :], ids_one_hot[q:q + 1, :].partition_broadcast(P)
                             ).then_inc(spread_ids_in[q % IDS_RING], 16)

            sp.dma_start(gather_ids[:], ids_gather).then_inc(gather_ids_in, 16)
            for q in range(NQ):
                load_spread_ids(q)
                if q == 0:
                    sp.dma_start(consts[:], small).then_inc(consts_in, 16)
                load_table(q)
                if q == 1:
                    sp.dma_start(dense[:], dense_t).then_inc(dense_in, 16)
                if q == 3:
                    sp.dma_start(w_dense_parts[:], w_dense).then_inc(w_dense_in, 16)
                if q == 4:
                    sp.dma_start(w_pairs_sb[:], w_pairs).then_inc(w_pairs_in, 16)
                    sp.dma_start(w2_sb[:], w2).then_inc(w2_in, 16)
            sp.wait_ge(y_ready, TILES)
            sp.dma_start(out, y[:]).then_inc(out_written, 16)
            sp.wait_ge(out_written, 16)

        @block.gpsimd
        def _(pool):
            pool.wait_ge(gather_ids_in, 16)
            for t in range(TILES):
                for lot, members in enumerate(GATHER_LOTS):
                    for k in members:
                        at = t * NG + k
                        pool.indirect_dma_start(
                            out=gathered[:, t, k, :], out_offset=None, in_=tables[GATHERED[k]],
                            in_offset=bass.IndirectOffsetOnAxis(ap=gather_ids[:, at:at + 1], axis=0),
                        ).then_inc(rows_in[t][lot], 16)

        def fill_copy(k):
            kind, *of = FILLS[k]
            if kind == "one_hot":
                return columns[:, :, 1 + of[0]], fill_bank[bank_of(k)][:, :]
            t, lot = of
            members = GATHER_LOTS[lot]
            slot = 1 + NQ + members[0]
            src = fill_bank[bank_of(k)][:, 0:len(members) * TILE].rearrange("p (f n) -> p n f", n=TILE)
            return columns[:, t * TILE:(t + 1) * TILE, slot:slot + len(members)], src

        def gram_copy(half):
            src = gram_bank[half][:, 0:HALF_GROUPS * SLOTS].rearrange("p (g j) -> p j g", j=SLOTS)
            return gram[:, :, half * HALF_GROUPS:(half + 1) * HALF_GROUPS], src

        def turn_copy(b, jq):
            at = (jq - TURN_LOTS[b][0]) * P
            src = turn_bank[b][0:TURNED, at:at + P].rearrange("p (s i) -> p s i", i=QUADRANT)
            return half_turned[:, :, PAIR_AT[jq]:PAIR_AT[jq] + KEPT[jq]], src[:, :, 0:KEPT[jq]]

        @block.scalar
        def _(act):
            copy = nc.scalar.copy
            act.wait_ge(warm_ready, 1)
            nc.scalar.activation(warm_out[:], warm[:, 0:1], ACT.Identity)

            def shift(q):
                act.wait_ge(spread_ids_in[q % IDS_RING], 16 * (q // IDS_RING + 1))
                if q >= SPLIT_RING:
                    act.wait_ge(one_hot_ready, CHUNKS * (q - SPLIT_RING + 1))
                nc.scalar.activation(shifted_ids[0:ROW_PARTS, q % SPLIT_RING],
                                     spread_ids[0:ROW_PARTS, q % IDS_RING], ACT.Identity,
                                     bias=consts[0:ROW_PARTS, C_BASE:C_BASE + 1]).then_inc(shifted_ready, 1)

            def split_hi(q):
                act.wait_ge(table_in[q % RAW_RING], 32 * (q // RAW_RING + 1))
                if q >= SPLIT_RING:
                    act.wait_ge(fill_done, fills_with(q - SPLIT_RING))
                copy(table_hi[0:ROW_PARTS, q % SPLIT_RING],
                     table_raw[0:ROW_PARTS, q % RAW_RING]).then_inc(hi_ready, 1)

            act.wait_ge(consts_in, 16)
            for q in range(2):
                shift(q)
                split_hi(q)
            act.wait_ge(dense_in, 16)
            copy(columns[:, :, 0], dense[:]).then_inc(dense_slot_ready, 1)

            for stage, *of in STAGES:
                if stage in ("one_hot", "gather"):
                    k = FILLS.index((stage, *of))
                    ahead = of[0] + 2 if stage == "one_hot" and of[0] + 2 < NQ else None
                    if ahead is not None:
                        shift(ahead)
                    if copier(k) == "act":
                        act.wait_ge(fill_done, k + 1)
                        copy(*fill_copy(k)).then_inc(copied["act"], 1)
                    if ahead is not None:
                        split_hi(ahead)
                elif stage == "gram" and of[1] == 0:
                    act.wait_ge(gram_done, 2 * of[0] + 1)
                    copy(*gram_copy(0)).then_inc(gram_copied[0], 1)
                elif stage == "first_turn":
                    for b in (0, 2):
                        act.wait_ge(turn_done[b], of[0] + 1)
                        for jq in TURN_LOTS[b]:
                            last = copy(*turn_copy(b, jq))
                        last.then_inc(turn_copied[b], 1)
                elif stage == "layer1" and of[1] == 0:
                    act.wait_ge(layer1_done, 2 * of[0] + 1)
                    for m in range(HALF_BLOCKS1):
                        last = nc.scalar.activation(
                            hidden1[:, m, :], layer1_bank[0][:, m * TILE:(m + 1) * TILE], ACT.Relu,
                            bias=consts[:, C_B1 + m:C_B1 + m + 1])
                    last.then_inc(hidden1_ready[0], 1)
                elif stage == "layer2" and of[1] == 0:
                    act.wait_ge(layer2_done, 2 * of[0] + 1)
                    nc.scalar.activation(hidden2[:, 0, :], layer2_bank[of[0]][0][:, 0:TILE], ACT.Relu,
                                         bias=consts[:, C_B2:C_B2 + 1]).then_inc(hidden2_ready[0], 1)
                elif stage == "layer3":
                    act.wait_ge(layer3_done, of[0] + 1)
                    copy(y[:, of[0]:of[0] + 1], layer_bank[:, 0:1]).then_inc(y_ready, 1)

        @block.vector
        def _(dve):
            copy = nc.vector.tensor_copy
            nc.vector.memset(warm[:], 0.0).then_inc(warm_ready, 1)
            for half in range(2):
                nc.vector.memset(gram_bank[half][:], 0.0).then_inc(gram_pads_ready, 1)
            for q in range(NQ):
                dve.wait_ge(shifted_ready, q + 1)
                if q >= ONE_HOT_RING:
                    dve.wait_ge(fill_done, fills_with(q - ONE_HOT_RING))
                for c in range(CHUNKS):
                    nc.vector.tensor_scalar(
                        one_hot[0:ROW_PARTS, q % ONE_HOT_RING, c, :], shifted_ids[0:ROW_PARTS, q % SPLIT_RING],
                        float(c), None, ALU.is_equal).then_inc(one_hot_ready, 1)
                dve.wait_ge(hi_ready, q + 1)
                nc.vector.tensor_tensor(
                    table_lo[0:ROW_PARTS, q % SPLIT_RING], table_raw[0:ROW_PARTS, q % RAW_RING],
                    table_hi[0:ROW_PARTS, q % SPLIT_RING].bitcast(f32), ALU.subtract).then_inc(lo_ready, 1)
            dve.wait_ge(consts_in, 16)
            dve.wait_ge(w_dense_in, 16)
            nc.vector.tensor_tensor(w_dense_sum[:], w_dense_parts[:, 0, :], w_dense_parts[:, 1, :],
                                    ALU.add).then_inc(w_dense_ready, 1)

            for stage, *of in STAGES:
                if stage in ("one_hot", "gather"):
                    k = FILLS.index((stage, *of))
                    if copier(k) == "dve":
                        dve.wait_ge(fill_done, k + 1)
                        copy(*fill_copy(k)).then_inc(copied["dve"], 1)
                elif stage == "gram" and of[1] == 1:
                    dve.wait_ge(gram_done, 2 * of[0] + 2)
                    copy(*gram_copy(1)).then_inc(gram_copied[1], 1)
                elif stage == "first_turn":
                    dve.wait_ge(turn_done[1], of[0] + 1)
                    for jq in TURN_LOTS[1]:
                        last = copy(*turn_copy(1, jq))
                    last.then_inc(turn_copied[1], 1)
                elif stage == "layer1" and of[1] == 1:
                    dve.wait_ge(layer1_done, 2 * of[0] + 2)
                    for m in range(HALF_BLOCKS1):
                        at = HALF_BLOCKS1 + m
                        last = nc.vector.tensor_scalar(
                            hidden1[:, at, :], layer1_bank[1][:, m * TILE:(m + 1) * TILE],
                            consts[:, C_B1 + at:C_B1 + at + 1], 0.0, ALU.add, ALU.max)
                    last.then_inc(hidden1_ready[1], 1)
                elif stage == "layer2" and of[1] == 1:
                    dve.wait_ge(layer2_done, 2 * of[0] + 2)
                    nc.vector.tensor_scalar(hidden2[:, 1, :], layer2_bank[of[0]][1][:, 0:TILE],
                                            consts[:, C_B2 + 1:C_B2 + 2], 0.0, ALU.add,
                                            ALU.max).then_inc(hidden2_ready[1], 1)
                elif stage == "second_turn":
                    dve.wait_ge(pairs_done, of[0] + 1)
                    copy(pairs[:].rearrange("c j (s g) -> c s j g", g=GROUPS),
                         pairs_bank[0:PAIR_ROWS, 0:SAMPLES_AT_ONCE * TURNED].rearrange(
                             "c (s j g) -> c s j g", s=SAMPLES_AT_ONCE, g=GROUPS)).then_inc(pairs_copied, 1)

        @block.tensor
        def _(pe):
            def bank_free(k):
                n = before_in_bank(k)
                if n is not None:
                    pe.wait_ge(copied[copier(n)], copies_until(copier(n), n))

            def multiply_table(k, q):
                bank_free(k)
                pe.wait_ge(hi_ready, q + 1)
                for c in range(CHUNKS):
                    pe.wait_ge(one_hot_ready, q * CHUNKS + c + 1)
                    nc.tensor.matmul(fill_bank[bank_of(k)][:], table_hi[0:ROW_PARTS, q % SPLIT_RING, c, :],
                                     one_hot[0:ROW_PARTS, q % ONE_HOT_RING, c, :],
                                     start=(c == 0), stop=False)
                pe.wait_ge(lo_ready, q + 1)
                for c in range(CHUNKS):
                    last = nc.tensor.matmul(fill_bank[bank_of(k)][:], table_lo[0:ROW_PARTS, q % SPLIT_RING, c, :],
                                            one_hot[0:ROW_PARTS, q % ONE_HOT_RING, c, :],
                                            start=False, stop=(c == CHUNKS - 1))
                last.then_inc(fill_done, 1)

            def turn_rows(k, t, lot):
                bank_free(k)
                members = GATHER_LOTS[lot]
                if t == 0 and lot == 0:
                    pe.wait_ge(consts_in, 16)
                pe.wait_ge(rows_in[t][lot], 16 * len(members))
                for n, f in enumerate(members):
                    last = nc.tensor.transpose(fill_bank[bank_of(k)][:, n * TILE:(n + 1) * TILE],
                                               gathered[:, t, f, :], ident)
                last.then_inc(fill_done, 1)

            def dot_products(t, half):
                if t == 0 and half == 0:
                    pe.wait_ge(dense_slot_ready, 1)
                    pe.wait_ge(gram_pads_ready, 2)
                if half == 0:
                    for who in ("act", "dve"):
                        count = copies_until(who, last_fill_of(t))
                        if count:
                            pe.wait_ge(copied[who], count)
                if t:
                    pe.wait_ge(gram_copied[half], t)
                    if half == 0:
                        pe.wait_ge(turn_copied[2], t)
                    elif t > 1:
                        pe.wait_ge(hidden2_ready[0], t - 1)
                for g in range(HALF_GROUPS):
                    for s in range(SAMPLES_AT_ONCE):
                        n = t * TILE + s * GROUPS + half * HALF_GROUPS + g
                        last = nc.tensor.matmul(
                            gram_bank[half][s * QUADRANT:s * QUADRANT + SLOTS, g * SLOTS:(g + 1) * SLOTS],
                            columns[:, n, :], columns[:, n, :], start=True, stop=True)
                last.then_inc(gram_done, 1)

            def first_turn(t):
                for half in range(2):
                    pe.wait_ge(gram_copied[half], t + 1)
                if t == 0:
                    for who in ("act", "dve"):
                        pe.wait_ge(copied[who], copies_until(who, EARLY_FILLS - 1))
                else:
                    pe.wait_ge(hidden1_ready[0], t)
                    if t == TILES - 2:
                        pe.wait_ge(hidden2_ready[1], t - 1)
                for b, lot in enumerate(TURN_LOTS):
                    for n, jq in enumerate(lot):
                        last = nc.tensor.transpose(
                            turn_bank[b][0:TURNED, n * P:(n + 1) * P],
                            gram[:, JLOW * jq:JLOW * (jq + 1), :].rearrange("p j g -> p (j g)"), ident)
                    last.then_inc(turn_done[b], 1)

            def second_turn(t):
                for b in range(len(TURN_LOTS)):
                    pe.wait_ge(turn_copied[b], t + 1)
                for s in range(SAMPLES_AT_ONCE):
                    last = nc.tensor.transpose(pairs_bank[0:PAIR_ROWS, s * TURNED:(s + 1) * TURNED],
                                               half_turned[:, s, :], ident[0:TURNED, 0:TURNED])
                last.then_inc(pairs_done, 1)

            def layer1(t, half):
                if half == 0:
                    if t == 0:
                        pe.wait_ge(w_dense_ready, 1)
                        pe.wait_ge(w_pairs_in, 16)
                elif t:
                    pe.wait_ge(y_ready, t)
                for m in range(HALF_BLOCKS1):
                    units = slice((half * HALF_BLOCKS1 + m) * P, (half * HALF_BLOCKS1 + m + 1) * P)
                    sums = layer1_bank[half][:, m * TILE:(m + 1) * TILE]
                    nc.tensor.matmul(sums, w_dense_sum[:, units], dense[:, t * TILE:(t + 1) * TILE],
                                     start=True, stop=False)
                    if half == 0 and m == 0:
                        pe.wait_ge(pairs_copied, t + 1)
                    for jj in range(JLOW):
                        last = nc.tensor.matmul(sums, w_pairs_sb[:, jj, units], pairs[:, jj, :],
                                                start=False, stop=(jj == JLOW - 1))
                last.then_inc(layer1_done, 1)

            def layer2(t, half):
                if t == 0 and half == 0:
                    pe.wait_ge(w2_in, 16)
                if t == TILES - 1:
                    pe.wait_ge(hidden2_ready[half], t)
                for k in range(UNIT_BLOCKS1):
                    if half == 0 and k % HALF_BLOCKS1 == 0:
                        pe.wait_ge(hidden1_ready[k // HALF_BLOCKS1], t + 1)
                    last = nc.tensor.matmul(layer2_bank[t][half][:, 0:TILE],
                                            w2_sb[:, k, half * P:(half + 1) * P], hidden1[:, k, :],
                                            start=(k == 0), stop=(k == UNIT_BLOCKS1 - 1))
                last.then_inc(layer2_done, 1)

            def layer3(t):
                for k in range(UNIT_BLOCKS2):
                    pe.wait_ge(hidden2_ready[k], t + 1)
                    last = nc.tensor.matmul(layer_bank[:, 0:1], hidden2[:, k, :],
                                            consts[:, C_W3 + k:C_W3 + k + 1],
                                            start=(k == 0), stop=(k == UNIT_BLOCKS2 - 1))
                last.then_inc(layer3_done, 1)

            pe.wait_ge(warm_ready, 1)
            for _ in range(WARM_PRODUCTS):
                nc.tensor.matmul(pairs_bank[:], warm[:, 0:P], warm[:], start=True, stop=True)

            for stage, *of in STAGES:
                if stage == "one_hot":
                    multiply_table(FILLS.index((stage, *of)), *of)
                elif stage == "gather":
                    turn_rows(FILLS.index((stage, *of)), *of)
                elif stage == "gram":
                    dot_products(*of)
                elif stage == "first_turn":
                    first_turn(*of)
                elif stage == "second_turn":
                    second_turn(*of)
                elif stage == "layer1":
                    layer1(*of)
                elif stage == "layer2":
                    layer2(*of)
                elif stage == "layer3":
                    layer3(*of)


def kernel(**inputs):
    import concourse.bacc as bacc
    from concourse.bass_utils import run_bass_kernel_spmd

    x = {name: np.ascontiguousarray(a) for name, a in inputs.items()}
    ids = x["ids"]
    w1 = x["W_top1"]
    padded = np.concatenate([w1, np.zeros((1, HIDDEN1), w1.dtype)])
    small = np.zeros((P, C_END), np.float32)
    small[:, C_IDENT:C_IDENT + P] = np.eye(P, dtype=np.float32)
    small[:, C_BASE] = np.arange(P) * -CHUNKS
    small[:, C_B1:C_B2] = x["b_top1"].reshape(-1, P).T
    small[:, C_B2:C_W3] = x["b_top2"].reshape(-1, P).T
    small[:, C_W3:C_END] = x["W_top3"].reshape(-1, P).T
    arrays = {
        "ids_gather": ids[:, GATHERED].reshape(TILES, TILE, NG).transpose(1, 0, 2).reshape(P, TILES * NG),
        "ids_one_hot": ids[:, ONE_HOT].T,
        "dense_t": x["r_dense_features"].T,
        "w_pairs": padded[pair_rows()],
        "w_dense": np.stack([w1[0:D], w1[-D:]], axis=1),
        "w2": x["W_top2"].reshape(UNIT_BLOCKS1, P, HIDDEN2).transpose(1, 0, 2),
        "small": small,
    }
    arrays |= {f"tbl_{f}": x[f"tbl_{f}"] for f in range(TABLES)}
    arrays = {name: np.ascontiguousarray(a) for name, a in arrays.items()}

    nc = bacc.Bacc("TRN2", target_bir_lowering=False, num_devices=1)
    d = {name: nc.dram_tensor(name, a.shape, mybir.dt.from_np(a.dtype), kind="ExternalInput").ap()
         for name, a in arrays.items()}
    out = nc.dram_tensor("out", (P, TILES), mybir.dt.float32, kind="ExternalOutput").ap()
    dlrm_tower(nc, d["ids_gather"], d["ids_one_hot"], d["dense_t"],
               [d[f"tbl_{f}"] for f in range(TABLES)], d["w_pairs"], d["w_dense"], d["w2"], d["small"], out)
    r = run_bass_kernel_spmd(nc, [arrays], core_ids=[0])
    return np.ascontiguousarray(r.results[0]["out"].T).reshape(BATCH, 1)
```

```python
from contextlib import ExitStack

import numpy as np
import concourse.bass as bass
from concourse import mybir

P = 128
BATCH = 512
D = 128
TABLES = 26
ROWS = [1000, 125000, 1250, 12500, 1000, 1250, 1250, 12500, 1000, 1000, 1000, 1000, 1250,
        1000, 1000, 12500, 12500, 1250, 1000, 1250, 1250, 12500, 1250, 12500, 1000, 1250]
FEATURES = TABLES + 1
HIDDEN1, HIDDEN2 = 512, 256
UNIT_BLOCKS1, UNIT_BLOCKS2 = HIDDEN1 // P, HIDDEN2 // P
HALF_BLOCKS1 = UNIT_BLOCKS1 // 2

SHORT = min(ROWS)
WHOLE, PARTIAL_FROM = 9, 2
ONE_HOT = [f for f in range(TABLES) if ROWS[f] == SHORT][:WHOLE + 1]
PARTIAL = ONE_HOT[WHOLE]
GATHERED = [PARTIAL] + [f for f in range(TABLES) if f not in ONE_HOT]
ROW_PARTS = 125
CHUNKS = SHORT // ROW_PARTS
NQ, NG = len(ONE_HOT), len(GATHERED)

TILE = P
TILES = BATCH // TILE
SLOTS = FEATURES
FEATURE_OF_SLOT = [0] + [f + 1 for f in ONE_HOT[:WHOLE]] + [f + 1 for f in GATHERED]

SAMPLES_AT_ONCE = 4
QUADRANT = P // SAMPLES_AT_ONCE
GROUPS = TILE // SAMPLES_AT_ONCE
HALF_GROUPS = GROUPS // 2
JLOW = 3
JQ = SLOTS // JLOW
KEPT = [JLOW * (jq + 1) - 1 for jq in range(JQ)]
PAIR_AT = [sum(KEPT[:jq]) for jq in range(JQ)]
PAIR_ROWS = sum(KEPT)
GATHERS_PER_BANK = 4
EARLY_LOTS = [range(k, min(k + GATHERS_PER_BANK, NG)) for k in range(0, NG, GATHERS_PER_BANK)]
LATE_LOTS = [range(k, min(k + GATHERS_PER_BANK, NG)) for k in range(1, NG, GATHERS_PER_BANK)]
LAST_LOTS = LATE_LOTS[:-1] + [LATE_LOTS[-1][:-1], LATE_LOTS[-1][-1:]]
GATHER_LOTS = [EARLY_LOTS if t < PARTIAL_FROM else LATE_LOTS if t < TILES - 1 else LAST_LOTS for t in range(TILES)]

FILL_BANKS = 3
SPLIT_JQ = 6
OUTPUTS_AT = HALF_BLOCKS1 * TILE
WARM_PRODUCTS = 13
RAW_RING, SPLIT_RING, ONE_HOT_RING, IDS_RING = 3, 2, 2, 3

C_IDENT, C_BASE, C_B1, C_B2, C_W3 = 0, P, P + 1, P + 5, P + 7
C_END = C_W3 + 2


def pair_rows():
    rows = np.full((PAIR_ROWS, JLOW), -1)
    for jq in range(JQ):
        for jj in range(JLOW):
            j = JLOW * jq + jj
            for i in range(j):
                a, b = sorted((FEATURE_OF_SLOT[i], FEATURE_OF_SLOT[j]))
                rows[PAIR_AT[jq] + i, jj] = D + a * (FEATURES - 1) - a * (a - 1) // 2 + b - a - 1
    return rows


def stages():
    def fills(t, lots):
        return [("gather", t, lot) for lot in lots if lot < len(GATHER_LOTS[t])]

    def layer1(t, *blocks):
        return [("layer1", t, m) for m in blocks]

    lots = range(max(len(lots) for lots in GATHER_LOTS))
    order = []
    early = fills(0, lots) + fills(1, lots)
    for q in range(WHOLE):
        order.append(("one_hot", q))
        if q >= 1:
            order.append(early.pop(0))
    order.append(early.pop(0))
    order += [("gram", 0, 0), ("gram", 0, 1), *early, ("one_hot", WHOLE), *fills(2, lots[:1]), ("turn", 0)]
    order += [("gram", 1, 0), *fills(2, lots[1:2]), *layer1(0, 0, 1),
              ("gram", 1, 1), *layer1(0, 2, 3), *fills(2, lots[2:3]),
              ("turn", 1), ("layer2", 0, 0), *fills(2, lots[3:]), ("layer2", 0, 1)]
    order += [("gram", 2, 0), *layer1(1, 0, 1),
              ("gram", 2, 1), *layer1(1, 2, 3), *fills(3, lots[:1]),
              ("turn", 2), ("layer2", 1, 0), *fills(3, lots[1:2]), ("layer2", 1, 1), *fills(3, lots[2:3]),
              *layer1(2, 0, 1), ("layer3", 0), *layer1(2, 2), *fills(3, lots[3:]), *layer1(2, 3)]
    order += [("gram", 3, 0), ("gram", 3, 1), ("layer2", 2, 0), ("layer2", 2, 1), ("dense", 3, 0),
              ("turn", 3), ("dense", 3, 1), ("dense", 3, 2), ("layer3", 1),
              *layer1(3, 0, 1, 2, 3), ("layer2_both", 3), ("layer3", 2), ("layer3", 3)]
    return order


STAGES = stages()
FILLS = [s for s in STAGES if s[0] in ("one_hot", "gather")]


def first_sample(q):
    return 0 if q < WHOLE else PARTIAL_FROM * TILE


def fills_with(q):
    return FILLS.index(("one_hot", q)) + 1


def copier(k):
    at = STAGES.index(FILLS[k])
    before = [s[0] for s in STAGES[:at] if s[0] in ("gram", "turn")]
    return "dve" if before and before[-1] == "turn" and k % 2 else "act"


def copies_until(engine, last):
    return sum(copier(k) == engine for k in range(last + 1))


def before_in_bank(k):
    return k - FILL_BANKS if k >= FILL_BANKS else None


def last_fill_of(tile):
    return max(k for k, f in enumerate(FILLS)
               if f[0] == "gather" and f[1] == tile or f[0] == "one_hot" and first_sample(f[1]) <= tile * TILE)


def dlrm_tower(nc, ids_gather, ids_one_hot, dense_t, tables, w_pairs, w_dense, w2, small, out):
    f32, f32r, i32 = mybir.dt.float32, mybir.dt.float32r, mybir.dt.int32
    ALU = mybir.AluOpType
    ACT = mybir.ActivationFunctionType

    with ExitStack() as ctx:
        def sb(name, shape, dtype=f32):
            return ctx.enter_context(nc.sbuf_tensor(name, shape, dtype))

        def bank(name):
            return ctx.enter_context(nc.psum_tensor(name, [P, 512], f32))

        def sem(name):
            return ctx.enter_context(nc.semaphore(name))

        gather_ids = sb("gather_ids", [P, TILES * NG], i32)
        gathered = sb("gathered", [P, TILES, NG, D])
        spread_ids = sb("spread_ids", [P, IDS_RING, BATCH], i32)
        shifted_ids = sb("shifted_ids", [P, SPLIT_RING, BATCH])
        table_raw = sb("table_raw", [P, RAW_RING, CHUNKS, D])
        table_hi = sb("table_hi", [P, SPLIT_RING, CHUNKS, D], f32r)
        table_lo = sb("table_lo", [P, SPLIT_RING, CHUNKS, D], f32r)
        one_hot = sb("one_hot", [P, ONE_HOT_RING, CHUNKS, BATCH], f32r)
        dense = sb("dense", [P, BATCH])
        columns = sb("columns", [P, BATCH, SLOTS])
        gram = sb("gram", [P, SLOTS, QUADRANT])
        packed = sb("packed", [P, JLOW, PAIR_ROWS])
        pairs = sb("pairs", [PAIR_ROWS, JLOW, TILE])
        w_pairs_sb = sb("w_pairs_sb", [PAIR_ROWS, JLOW, HIDDEN1])
        w_dense_parts = sb("w_dense_parts", [P, 2, HIDDEN1])
        w_dense_sum = sb("w_dense_sum", [P, HIDDEN1])
        w2_sb = sb("w2_sb", [P, UNIT_BLOCKS1, HIDDEN2])
        hidden1 = sb("hidden1", [P, UNIT_BLOCKS1, TILE])
        hidden2 = sb("hidden2", [P, 2, UNIT_BLOCKS2, TILE])
        consts = sb("consts", [P, C_END])
        warm = sb("warm", [P, BATCH], mybir.dt.bfloat16)
        warm_out = sb("warm_out", [P, 1])
        y = sb("y", [P, TILES])
        ident = consts[:, C_IDENT:C_IDENT + P]

        fill_bank = [bank(f"fill_bank{b}") for b in range(FILL_BANKS)]
        gram_banks = ctx.enter_context(nc.psum_tensor("gram_banks", [P, 2, 512], f32))
        pairs_bank = bank("pairs_bank")
        layer_bank = [bank("layer_bank0"), bank("layer_bank1")]

        def layer1_sums(t, m):
            if t == TILES - 1:
                return [*fill_bank, layer_bank[0]][m][:, 0:TILE]
            half, at = divmod(m, HALF_BLOCKS1)
            return layer_bank[half][:, at * TILE:(at + 1) * TILE]

        def dense_ahead(t, m):
            return ("dense", t, m) in STAGES

        def layer2_sums(t, half):
            if t == TILES - 1:
                return gram_banks[:, half, 0:TILE]
            return layer_bank[half][:, 0:TILE]

        def packed_by(who, t):
            helped = t == TILES - 1
            if who == "act":
                return range(SPLIT_JQ, JQ) if helped else range(0)
            return range(SPLIT_JQ if helped else JQ)

        def bank_complete(t, m):
            if t == TILES - 1:
                return [m]
            return [m - 1, m] if m % HALF_BLOCKS1 == 1 else []

        gather_ids_in = sem("gather_ids_in")
        consts_in = sem("consts_in")
        dense_in = sem("dense_in")
        spread_ids_in = [sem(f"spread_ids_in{r}") for r in range(IDS_RING)]
        table_in = [sem(f"table_in{r}") for r in range(RAW_RING)]
        rows_in = [[sem(f"rows_in{t}_{lot}") for lot in range(len(GATHER_LOTS[t]))] for t in range(TILES)]
        w_pairs_in = sem("w_pairs_in")
        w_dense_in = sem("w_dense_in")
        w2_in = sem("w2_in")
        warm_ready = sem("warm_ready")
        shifted_ready = sem("shifted_ready")
        hi_ready = sem("hi_ready")
        lo_ready = sem("lo_ready")
        one_hot_ready = sem("one_hot_ready")
        fill_done = sem("fill_done")
        copied = {"act": sem("copied_by_act"), "dve": sem("copied_by_dve")}
        dense_slot_ready = sem("dense_slot_ready")
        gram_pads_ready = sem("gram_pads_ready")
        gram_done = sem("gram_done")
        gram_turned = sem("gram_turned")
        pairs_packed = sem("pairs_packed")
        packed_by_act = sem("packed_by_act")
        pairs_done = sem("pairs_done")
        pairs_copied = sem("pairs_copied")
        w_dense_ready = sem("w_dense_ready")
        layer1_done = sem("layer1_done")
        hidden1_ready = [sem("hidden1_ready0"), sem("hidden1_ready1")]
        layer2_done = sem("layer2_done")
        hidden2_ready = [sem("hidden2_ready0"), sem("hidden2_ready1")]
        layer3_done = sem("layer3_done")
        y_ready = sem("y_ready")
        out_written = sem("out_written")

        block = ctx.enter_context(nc.Block())

        @block.sync
        def _(sp):
            def load_table(q):
                table = tables[ONE_HOT[q]].rearrange("(p c) d -> p (c d)", c=CHUNKS)
                even = ROW_PARTS // 16 * 16
                dst = table_raw[:, q % RAW_RING].rearrange("p c d -> p (c d)")
                if q >= RAW_RING:
                    sp.wait_ge(lo_ready, q - RAW_RING + 1)
                sp.dma_start(dst[0:even, :], table[0:even, :]).then_inc(table_in[q % RAW_RING], 16)
                sp.dma_start(dst[even:ROW_PARTS, :],
                             table[even:ROW_PARTS, :]).then_inc(table_in[q % RAW_RING], 16)

            def load_spread_ids(q):
                if q >= IDS_RING:
                    sp.wait_ge(shifted_ready, q - IDS_RING + 1)
                sp.dma_start(spread_ids[:, q % IDS_RING, :], ids_one_hot[q:q + 1, :].partition_broadcast(P)
                             ).then_inc(spread_ids_in[q % IDS_RING], 16)

            sp.dma_start(gather_ids[:], ids_gather).then_inc(gather_ids_in, 16)
            load_spread_ids(0)
            sp.dma_start(consts[:], small).then_inc(consts_in, 16)
            for q in range(NQ):
                load_table(q)
                if q + 1 < NQ:
                    load_spread_ids(q + 1)
            sp.dma_start(dense[:], dense_t).then_inc(dense_in, 16)
            sp.dma_start(w_dense_parts[:], w_dense).then_inc(w_dense_in, 16)
            sp.wait_ge(gram_done, 1)
            sp.dma_start(w_pairs_sb[:], w_pairs).then_inc(w_pairs_in, 16)
            sp.dma_start(w2_sb[:], w2).then_inc(w2_in, 16)
            sp.wait_ge(y_ready, 1)
            sp.dma_start(out, y[:]).then_inc(out_written, 16)
            sp.wait_ge(out_written, 16)

        @block.gpsimd
        def _(pool):
            pool.wait_ge(gather_ids_in, 16)
            for t in range(TILES):
                for lot, members in enumerate(GATHER_LOTS[t]):
                    for k in members:
                        at = t * NG + k
                        pool.indirect_dma_start(
                            out=gathered[:, t, k, :], out_offset=None, in_=tables[GATHERED[k]],
                            in_offset=bass.IndirectOffsetOnAxis(ap=gather_ids[:, at:at + 1], axis=0),
                        ).then_inc(rows_in[t][lot], 16)

        def fill_copy(k):
            kind, *of = FILLS[k]
            if kind == "one_hot":
                first = first_sample(of[0])
                return columns[:, first:, 1 + of[0]], fill_bank[k % FILL_BANKS][:, 0:BATCH - first]
            t, lot = of
            members = GATHER_LOTS[t][lot]
            slot = 1 + WHOLE + members[0]
            src = fill_bank[k % FILL_BANKS][:, 0:len(members) * TILE].rearrange("p (f n) -> p n f", n=TILE)
            return columns[:, t * TILE:(t + 1) * TILE, slot:slot + len(members)], src

        @block.scalar
        def _(act):
            copy = nc.scalar.copy
            act.wait_ge(warm_ready, 1)
            nc.scalar.activation(warm_out[:], warm[:, 0:1], ACT.Identity)

            def shift(q):
                act.wait_ge(spread_ids_in[q % IDS_RING], 16 * (q // IDS_RING + 1))
                if q >= SPLIT_RING:
                    act.wait_ge(one_hot_ready, CHUNKS * (q - SPLIT_RING + 1))
                first = first_sample(q)
                nc.scalar.activation(shifted_ids[0:ROW_PARTS, q % SPLIT_RING, first:],
                                     spread_ids[0:ROW_PARTS, q % IDS_RING, first:], ACT.Identity,
                                     bias=consts[0:ROW_PARTS, C_BASE:C_BASE + 1]).then_inc(shifted_ready, 1)

            def split_hi(q):
                act.wait_ge(table_in[q % RAW_RING], 32 * (q // RAW_RING + 1))
                if q >= SPLIT_RING:
                    act.wait_ge(fill_done, fills_with(q - SPLIT_RING))
                copy(table_hi[0:ROW_PARTS, q % SPLIT_RING],
                     table_raw[0:ROW_PARTS, q % RAW_RING]).then_inc(hi_ready, 1)

            act.wait_ge(consts_in, 16)
            for q in range(2):
                shift(q)
                split_hi(q)

            for stage, *of in STAGES:
                if stage in ("one_hot", "gather"):
                    k = FILLS.index((stage, *of))
                    ahead = of[0] + 2 if stage == "one_hot" and of[0] + 2 < NQ else None
                    if ahead is not None:
                        shift(ahead)
                    if stage == "one_hot" and of[0] == WHOLE - 1:
                        act.wait_ge(dense_in, 16)
                        copy(columns[:, :, 0], dense[:]).then_inc(dense_slot_ready, 1)
                    if copier(k) == "act":
                        act.wait_ge(fill_done, k + 1)
                        copy(*fill_copy(k)).then_inc(copied["act"], 1)
                    if ahead is not None:
                        split_hi(ahead)
                elif stage == "gram" and of[1] == 1 and packed_by("act", of[0]):
                    act.wait_ge(gram_turned, of[0] + 1)
                    for jq in packed_by("act", of[0]):
                        last = copy(packed[:, :, PAIR_AT[jq]:PAIR_AT[jq] + KEPT[jq]],
                                    gram[:, JLOW * jq:JLOW * (jq + 1), 0:KEPT[jq]])
                    last.then_inc(packed_by_act, 1)
                elif stage == "turn":
                    act.wait_ge(pairs_done, of[0] + 1)
                    copy(pairs[:].rearrange("c j n -> c (j n)"),
                         pairs_bank[0:PAIR_ROWS, 0:JLOW * TILE]).then_inc(pairs_copied, 1)
                elif stage == "layer1" and of[1] < HALF_BLOCKS1:
                    t, m = of
                    for b in bank_complete(t, m):
                        act.wait_ge(layer1_done, UNIT_BLOCKS1 * t + m + 1)
                        nc.scalar.activation(hidden1[:, b, :], layer1_sums(t, b), ACT.Relu,
                                             bias=consts[:, C_B1 + b:C_B1 + b + 1]).then_inc(hidden1_ready[0], 1)
                elif stage == "layer2_both" or stage == "layer2" and of[1] == 0:
                    act.wait_ge(layer2_done, 2 * of[0] + 1)
                    nc.scalar.activation(hidden2[:, of[0] % 2, 0, :], layer2_sums(of[0], 0), ACT.Relu,
                                         bias=consts[:, C_B2:C_B2 + 1]).then_inc(hidden2_ready[0], 1)
            act.wait_ge(layer3_done, TILES)
            copy(y[:], layer_bank[1][:, OUTPUTS_AT:OUTPUTS_AT + TILES]).then_inc(y_ready, 1)

        @block.vector
        def _(dve):
            copy = nc.vector.tensor_copy
            nc.vector.memset(warm[:], 0.0).then_inc(warm_ready, 1)
            nc.vector.memset(gram_banks[:], 0.0).then_inc(gram_pads_ready, 1)

            def make_one_hot(q):
                dve.wait_ge(shifted_ready, q + 1)
                if q >= ONE_HOT_RING:
                    dve.wait_ge(fill_done, fills_with(q - ONE_HOT_RING))
                first = first_sample(q)
                for c in range(CHUNKS):
                    nc.vector.tensor_scalar(
                        one_hot[0:ROW_PARTS, q % ONE_HOT_RING, c, first:],
                        shifted_ids[0:ROW_PARTS, q % SPLIT_RING, first:],
                        float(c), None, ALU.is_equal).then_inc(one_hot_ready, 1)

            def split_lo(q):
                dve.wait_ge(hi_ready, q + 1)
                nc.vector.tensor_tensor(
                    table_lo[0:ROW_PARTS, q % SPLIT_RING], table_raw[0:ROW_PARTS, q % RAW_RING],
                    table_hi[0:ROW_PARTS, q % SPLIT_RING].bitcast(f32), ALU.subtract).then_inc(lo_ready, 1)

            make_one_hot(0)
            split_lo(0)
            for q in range(1, NQ):
                split_lo(q)
                make_one_hot(q)
            dve.wait_ge(consts_in, 16)
            dve.wait_ge(w_dense_in, 16)
            nc.vector.tensor_tensor(w_dense_sum[:], w_dense_parts[:, 0, :], w_dense_parts[:, 1, :],
                                    ALU.add).then_inc(w_dense_ready, 1)

            for stage, *of in STAGES:
                if stage in ("one_hot", "gather"):
                    k = FILLS.index((stage, *of))
                    if copier(k) == "dve":
                        dve.wait_ge(fill_done, k + 1)
                        copy(*fill_copy(k)).then_inc(copied["dve"], 1)
                elif stage == "gram" and of[1] == 1:
                    dve.wait_ge(gram_done, 2 * of[0] + 2)
                    nc.vector.transpose(
                        gram[:], gram_banks[:, :, 0:HALF_GROUPS * SLOTS].rearrange(
                            "p h (g j) -> p j h g", j=SLOTS)).then_inc(gram_turned, 1)
                    dve.wait_ge(gram_turned, of[0] + 1)
                    for jq in packed_by("dve", of[0]):
                        last = copy(packed[:, :, PAIR_AT[jq]:PAIR_AT[jq] + KEPT[jq]],
                                    gram[:, JLOW * jq:JLOW * (jq + 1), 0:KEPT[jq]])
                    last.then_inc(pairs_packed, 1)
                elif stage == "layer1" and of[1] >= HALF_BLOCKS1:
                    t, m = of
                    for b in bank_complete(t, m):
                        dve.wait_ge(layer1_done, UNIT_BLOCKS1 * t + m + 1)
                        nc.vector.tensor_scalar(
                            hidden1[:, b, :], layer1_sums(t, b), consts[:, C_B1 + b:C_B1 + b + 1], 0.0,
                            ALU.add, ALU.max).then_inc(hidden1_ready[1], 1)
                elif stage == "layer2_both" or stage == "layer2" and of[1] == 1:
                    dve.wait_ge(layer2_done, 2 * of[0] + 2)
                    nc.vector.tensor_scalar(hidden2[:, of[0] % 2, 1, :], layer2_sums(of[0], 1),
                                            consts[:, C_B2 + 1:C_B2 + 2], 0.0, ALU.add,
                                            ALU.max).then_inc(hidden2_ready[1], 1)

        @block.tensor
        def _(pe):
            def bank_free(k):
                n = before_in_bank(k)
                if n is not None:
                    pe.wait_ge(copied[copier(n)], copies_until(copier(n), n))

            def multiply_table(k, q):
                bank_free(k)
                first = first_sample(q)
                parts, chunks = (table_hi, table_lo), range(CHUNKS)
                products = ([(part, c) for part in parts for c in chunks] if q == 0 else
                            [(part, c) for c in chunks for part in parts])
                pe.wait_ge(hi_ready, q + 1)
                for n, (part, c) in enumerate(products):
                    if part is table_hi:
                        pe.wait_ge(one_hot_ready, q * CHUNKS + c + 1)
                    elif c == 0:
                        pe.wait_ge(lo_ready, q + 1)
                    last = nc.tensor.matmul(fill_bank[k % FILL_BANKS][:, 0:BATCH - first],
                                            part[0:ROW_PARTS, q % SPLIT_RING, c, :],
                                            one_hot[0:ROW_PARTS, q % ONE_HOT_RING, c, first:],
                                            start=(n == 0), stop=(n == len(products) - 1))
                last.then_inc(fill_done, 1)

            def turn_rows(k, t, lot):
                bank_free(k)
                members = GATHER_LOTS[t][lot]
                if t == 0 and lot == 0:
                    pe.wait_ge(consts_in, 16)
                pe.wait_ge(rows_in[t][lot], 16 * len(members))
                for n, f in enumerate(members):
                    last = nc.tensor.transpose(fill_bank[k % FILL_BANKS][:, n * TILE:(n + 1) * TILE],
                                               gathered[:, t, f, :], ident)
                last.then_inc(fill_done, 1)

            def dot_products(t, half):
                if t == 0 and half == 0:
                    pe.wait_ge(dense_slot_ready, 1)
                    pe.wait_ge(gram_pads_ready, 1)
                if half == 0:
                    for who in ("act", "dve"):
                        count = copies_until(who, last_fill_of(t))
                        if count:
                            pe.wait_ge(copied[who], count)
                if t and half == 0:
                    pe.wait_ge(gram_turned, t)
                for g in range(HALF_GROUPS):
                    for s in range(SAMPLES_AT_ONCE):
                        n = t * TILE + s * GROUPS + half * HALF_GROUPS + g
                        last = nc.tensor.matmul(
                            gram_banks[s * QUADRANT:s * QUADRANT + SLOTS, half, g * SLOTS:(g + 1) * SLOTS],
                            columns[:, n, :], columns[:, n, :], start=True, stop=True)
                last.then_inc(gram_done, 1)

            def turn_pairs(t):
                pe.wait_ge(pairs_packed, t + 1)
                if packed_by("act", t):
                    pe.wait_ge(packed_by_act, 1)
                if t:
                    pe.wait_ge(pairs_copied, t)
                for jj in range(JLOW):
                    last = nc.tensor.transpose(pairs_bank[0:PAIR_ROWS, jj * TILE:(jj + 1) * TILE],
                                               packed[:, jj, :], ident)
                last.then_inc(pairs_done, 1)

            def layer1_dense(t, m):
                if m == 0 and t == 0:
                    pe.wait_ge(w_dense_ready, 1)
                    pe.wait_ge(w_pairs_in, 16)
                half, at = divmod(m, HALF_BLOCKS1)
                if at == 0 and 0 < t < TILES - 1:
                    pe.wait_ge(hidden2_ready[half], t)
                if t == TILES - 1 and m == UNIT_BLOCKS1 - 1:
                    pe.wait_ge(hidden2_ready[0], t)
                nc.tensor.matmul(layer1_sums(t, m), w_dense_sum[:, m * P:(m + 1) * P],
                                 dense[:, t * TILE:(t + 1) * TILE], start=True, stop=False)

            def layer1(t, m):
                if not dense_ahead(t, m):
                    layer1_dense(t, m)
                if m == 0:
                    pe.wait_ge(pairs_copied, t + 1)
                for jj in range(JLOW):
                    last = nc.tensor.matmul(layer1_sums(t, m), w_pairs_sb[:, jj, m * P:(m + 1) * P],
                                            pairs[:, jj, :], start=False, stop=(jj == JLOW - 1))
                last.then_inc(layer1_done, 1)

            def layer2(t, halves):
                if t == 0 and halves[0] == 0:
                    pe.wait_ge(w2_in, 16)
                for k in range(UNIT_BLOCKS1):
                    if t == TILES - 1:
                        pe.wait_ge(hidden1_ready[k // HALF_BLOCKS1], HALF_BLOCKS1 * t + k % HALF_BLOCKS1 + 1)
                    elif halves[0] == 0 and k % HALF_BLOCKS1 == 0:
                        pe.wait_ge(hidden1_ready[k // HALF_BLOCKS1], HALF_BLOCKS1 * (t + 1))
                    for half in halves:
                        product = nc.tensor.matmul(layer2_sums(t, half), w2_sb[:, k, half * P:(half + 1) * P],
                                                   hidden1[:, k, :], start=(k == 0), stop=(k == UNIT_BLOCKS1 - 1))
                        if k == UNIT_BLOCKS1 - 1:
                            product.then_inc(layer2_done, 1)

            def layer3(t):
                pe.wait_ge(hidden2_ready[1], sum(s[0] == "layer2" and s[2] == 1
                                                 for s in STAGES[:STAGES.index(("layer3", t))]))
                for k in range(UNIT_BLOCKS2):
                    pe.wait_ge(hidden2_ready[k], t + 1)
                    last = nc.tensor.matmul(layer_bank[1][:, OUTPUTS_AT + t:OUTPUTS_AT + t + 1],
                                            hidden2[:, t % 2, k, :], consts[:, C_W3 + k:C_W3 + k + 1],
                                            start=(k == 0), stop=(k == UNIT_BLOCKS2 - 1))
                last.then_inc(layer3_done, 1)

            pe.wait_ge(warm_ready, 1)
            for _ in range(WARM_PRODUCTS):
                nc.tensor.matmul(pairs_bank[:], warm[:, 0:P], warm[:], start=True, stop=True)

            for stage, *of in STAGES:
                if stage == "one_hot":
                    multiply_table(FILLS.index((stage, *of)), *of)
                elif stage == "gather":
                    turn_rows(FILLS.index((stage, *of)), *of)
                elif stage == "gram":
                    dot_products(*of)
                elif stage == "turn":
                    turn_pairs(*of)
                elif stage == "dense":
                    layer1_dense(*of)
                elif stage == "layer1":
                    layer1(*of)
                elif stage == "layer2":
                    layer2(of[0], of[1:])
                elif stage == "layer2_both":
                    layer2(of[0], (0, 1))
                elif stage == "layer3":
                    layer3(*of)


def kernel(**inputs):
    import concourse.bacc as bacc
    from concourse.bass_utils import run_bass_kernel_spmd

    x = {name: np.ascontiguousarray(a) for name, a in inputs.items()}
    ids = x["ids"]
    w1 = x["W_top1"]
    padded = np.concatenate([w1, np.zeros((1, HIDDEN1), w1.dtype)])
    small = np.zeros((P, C_END), np.float32)
    small[:, C_IDENT:C_IDENT + P] = np.eye(P, dtype=np.float32)
    small[:, C_BASE] = np.arange(P) * -CHUNKS
    small[:, C_B1:C_B2] = x["b_top1"].reshape(-1, P).T
    small[:, C_B2:C_W3] = x["b_top2"].reshape(-1, P).T
    small[:, C_W3:C_END] = x["W_top3"].reshape(-1, P).T
    arrays = {
        "ids_gather": ids[:, GATHERED].reshape(TILES, TILE, NG).transpose(1, 0, 2).reshape(P, TILES * NG),
        "ids_one_hot": ids[:, ONE_HOT].T,
        "dense_t": x["r_dense_features"].T,
        "w_pairs": padded[pair_rows()],
        "w_dense": np.stack([w1[0:D], w1[-D:]], axis=1),
        "w2": x["W_top2"].reshape(UNIT_BLOCKS1, P, HIDDEN2).transpose(1, 0, 2),
        "small": small,
    }
    arrays |= {f"tbl_{f}": x[f"tbl_{f}"] for f in range(TABLES)}
    arrays = {name: np.ascontiguousarray(a) for name, a in arrays.items()}

    nc = bacc.Bacc("TRN2", target_bir_lowering=False, num_devices=1)
    d = {name: nc.dram_tensor(name, a.shape, mybir.dt.from_np(a.dtype), kind="ExternalInput").ap()
         for name, a in arrays.items()}
    out = nc.dram_tensor("out", (P, TILES), mybir.dt.float32, kind="ExternalOutput").ap()
    dlrm_tower(nc, d["ids_gather"], d["ids_one_hot"], d["dense_t"],
               [d[f"tbl_{f}"] for f in range(TABLES)], d["w_pairs"], d["w_dense"], d["w2"], d["small"], out)
    r = run_bass_kernel_spmd(nc, [arrays], core_ids=[0])
    return np.ascontiguousarray(r.results[0]["out"].T).reshape(BATCH, 1)
```
